# Optimizing a Trainium2 kernel written in Bass

```python
import numpy as np
import jax
import jax.numpy as jnp

def _softmax(x, axis=-1):
    return jax.nn.softmax(x, axis=axis)

def _gelu(x):
    return jax.nn.gelu(x, approximate=True)

def _silu(x):
    return jax.nn.silu(x)

def _sigmoid(x):
    return jax.nn.sigmoid(x)

def _layernorm(x, axis=-1, eps=1e-05):
    m = jnp.mean(x, axis=axis, keepdims=True)
    v = jnp.var(x, axis=axis, keepdims=True)
    return (x - m) / jnp.sqrt(v + eps)

def _scatter_add(tgt, idx, src, axis=0):
    return tgt.at[idx].add(src)

def _segment_sum(src, seg, n):
    return jax.ops.segment_sum(src, seg, n)
kernel_name = 'mk_conv_seq_d1_conv_nchw256_r4_849ad8'

def setup_inputs(seed: int=0):
    np.random.seed(seed)
    _w = jnp.asarray

    def _rec_inputs():
        import jax
        import jax.numpy as jnp
        _gk = jax.random.key(seed)
        x = -0.0003957 + 1 * jax.random.normal(jax.random.fold_in(_gk, 1), (16, 64, 56, 56), jnp.float32)
        return x
    x = _rec_inputs()

    def _L0_conv_setup():
        import jax, jax.numpy as jnp
        import numpy as np
        EPS = 1e-05
        CG_GROUPS = 4
        CG_ALPHA = 2.0

        def conv3x3(x, w, stride=1):
            return jax.lax.conv_general_dilated(x, w, window_strides=(stride, stride), padding=((1, 1), (1, 1)), dimension_numbers=('NCHW', 'OIHW', 'NCHW'))

        def qconv_cg(x, w, theta):
            cin = x.shape[1]
            base = cin // CG_GROUPS
            yp = conv3x3(x[:, :base], w[:, :base])
            yr = conv3x3(x[:, base:], w[:, base:])
            d = jax.nn.sigmoid(CG_ALPHA * (yp - theta[None, :, None, None]))
            return yp + d * yr

        def bn(x, gamma, beta, mean, var):
            inv = gamma * jax.lax.rsqrt(var + EPS)
            return x * inv[None, :, None, None] + (beta - mean * inv)[None, :, None, None]
        key = jax.random.key(seed)
        k0, k1, k2 = jax.random.split(key, 3)
        C = 64
        x = jax.random.normal(k0, (16, C, 56, 56), jnp.float32)
        scale = 1.0 / np.sqrt(C * 9)
        w_a = jax.random.normal(k1, (C, C, 3, 3), jnp.float32) * scale
        w_b = jax.random.normal(k2, (C, C, 3, 3), jnp.float32) * scale
        z = jnp.zeros((C,), jnp.float32)
        o = jnp.ones((C,), jnp.float32)
        return dict(x=x, w_a=w_a, theta_a=z, gamma_a=o, beta_a=z, mean_a=z, var_a=o, w_b=w_b, theta_b=z, gamma_b=o, beta_b=z, mean_b=z, var_b=o)
    _L0_conv_all = _L0_conv_setup()
    _L0_conv_in = {k: v for k, v in _L0_conv_all.items() if k in ('w_a', 'theta_a', 'gamma_a', 'beta_a', 'mean_a', 'var_a', 'w_b', 'theta_b', 'gamma_b', 'beta_b', 'mean_b', 'var_b')}
    del _L0_conv_all
    return {'x': x, 'L0_conv_w_a': _L0_conv_in['w_a'], 'L0_conv_theta_a': _L0_conv_in['theta_a'], 'L0_conv_gamma_a': _L0_conv_in['gamma_a'], 'L0_conv_beta_a': _L0_conv_in['beta_a'], 'L0_conv_mean_a': _L0_conv_in['mean_a'], 'L0_conv_var_a': _L0_conv_in['var_a'], 'L0_conv_w_b': _L0_conv_in['w_b'], 'L0_conv_theta_b': _L0_conv_in['theta_b'], 'L0_conv_gamma_b': _L0_conv_in['gamma_b'], 'L0_conv_beta_b': _L0_conv_in['beta_b'], 'L0_conv_mean_b': _L0_conv_in['mean_b'], 'L0_conv_var_b': _L0_conv_in['var_b']}

def reference(x, L0_conv_w_a, L0_conv_theta_a, L0_conv_gamma_a, L0_conv_beta_a, L0_conv_mean_a, L0_conv_var_a, L0_conv_w_b, L0_conv_theta_b, L0_conv_gamma_b, L0_conv_beta_b, L0_conv_mean_b, L0_conv_var_b):
    import jax
    import jax.numpy as jnp

    def _L0_conv_ref(x, w_a, theta_a, gamma_a, beta_a, mean_a, var_a, w_b, theta_b, gamma_b, beta_b, mean_b, var_b):
        import jax, jax.numpy as jnp
        import numpy as np
        EPS = 1e-05
        CG_GROUPS = 4
        CG_ALPHA = 2.0

        def conv3x3(x, w, stride=1):
            return jax.lax.conv_general_dilated(x, w, window_strides=(stride, stride), padding=((1, 1), (1, 1)), dimension_numbers=('NCHW', 'OIHW', 'NCHW'))

        def qconv_cg(x, w, theta):
            cin = x.shape[1]
            base = cin // CG_GROUPS
            yp = conv3x3(x[:, :base], w[:, :base])
            yr = conv3x3(x[:, base:], w[:, base:])
            d = jax.nn.sigmoid(CG_ALPHA * (yp - theta[None, :, None, None]))
            return yp + d * yr

        def bn(x, gamma, beta, mean, var):
            inv = gamma * jax.lax.rsqrt(var + EPS)
            return x * inv[None, :, None, None] + (beta - mean * inv)[None, :, None, None]
        h = jax.nn.relu(bn(qconv_cg(x, w_a, theta_a), gamma_a, beta_a, mean_a, var_a))
        h = bn(qconv_cg(h, w_b, theta_b), gamma_b, beta_b, mean_b, var_b)
        return jax.nn.relu(x + h)

    def _gn(v, G=32, eps=1e-05):
        B_, C_, H_, W_ = v.shape
        g = v.reshape(B_, G, C_ // G, H_, W_)
        m = jnp.mean(g, axis=(2, 3, 4), keepdims=True)
        s = jnp.var(g, axis=(2, 3, 4), keepdims=True)
        return ((g - m) / jnp.sqrt(s + eps)).reshape(v.shape)

    def _ln_c(v, eps=1e-06):
        m = jnp.mean(v, axis=1, keepdims=True)
        s = jnp.var(v, axis=1, keepdims=True)
        return (v - m) / jnp.sqrt(s + eps)

    def _ln_t(v, eps=1e-05):
        m = jnp.mean(v, axis=-1, keepdims=True)
        s = jnp.var(v, axis=-1, keepdims=True)
        return (v - m) / jnp.sqrt(s + eps)

    def _to_tokens(v):
        B_, C_, H_, W_ = v.shape
        return v.reshape(B_, C_, H_ * W_).transpose(0, 2, 1)

    def _from_tokens(t, like):
        B_, C_, H_, W_ = like.shape
        return t.transpose(0, 2, 1).reshape(B_, C_, H_, W_)
    x = _L0_conv_ref(x, L0_conv_w_a, L0_conv_theta_a, L0_conv_gamma_a, L0_conv_beta_a, L0_conv_mean_a, L0_conv_var_a, L0_conv_w_b, L0_conv_theta_b, L0_conv_gamma_b, L0_conv_beta_b, L0_conv_mean_b, L0_conv_var_b)
    return x

_drawn_inputs = setup_inputs


def setup_inputs(seed=0):
    import zlib

    import numpy as np

    out = dict(_drawn_inputs(seed))
    spreads = {'L0_conv_theta_a': (0.0, 0.428),
     'L0_conv_gamma_a': (1.0, 0.2),
     'L0_conv_beta_a': (0.0, 0.1),
     'L0_conv_mean_a': (0.0, 0.1),
     'L0_conv_var_a': (1.0, 0.2),
     'L0_conv_theta_b': (0.0, 0.352),
     'L0_conv_gamma_b': (1.0, 0.2),
     'L0_conv_beta_b': (0.0, 0.1),
     'L0_conv_mean_b': (0.0, 0.1),
     'L0_conv_var_b': (1.0, 0.2)}
    factors = {}
    for name, (base, spread) in spreads.items():
        noise = np.random.default_rng([zlib.crc32(name.encode()), seed]).standard_normal(out[name].shape)
        drawn = base * np.exp(spread * noise) if base else spread * noise
        out[name] = jnp.asarray(drawn.astype(out[name].dtype))
    for name, factor in factors.items():
        out[name] = (out[name] * factor).astype(out[name].dtype)
    return out
```

```python
from contextlib import ExitStack

import concourse.bass as bass
from concourse import mybir

ALU = mybir.AluOpType
ACT = mybir.ActivationFunctionType
F32 = mybir.dt.float32
F32R = mybir.dt.float32r

P = 128
EPS = 1e-5
ALPHA = 2.0
GROUPS = 4
TAPS = 3
RING = 4
BANK = 512


def gated_conv_pair_kernel(nc, x, w_a, theta_a, gamma_a, beta_a, mean_a, var_a,
                           w_b, theta_b, gamma_b, beta_b, mean_b, var_b, out):
    B, C, H, W = x.shape
    assert 2 * C == P and H % 8 == 0
    BASE = C // GROUPS
    MID = 2 * BASE
    SLOTS = H // 2
    HALF = SLOTS // 2
    BLK = HALF // 2
    N = BLK * W
    PADW = W + 2
    assert N <= BANK and 4 * MID == P and 8 * BASE == P

    with ExitStack() as ctx:
        def sb(name, shape, dt=F32):
            return ctx.enter_context(nc.sbuf_tensor(name, shape, dt))

        def sem(name):
            return ctx.enter_context(nc.semaphore(name))

        x_pair = sb("x_pair", [P, RING * SLOTS * W])
        h_pair = sb("h_pair", [P, SLOTS, W])
        win_mid = [sb(f"win_mid{k}", [P, SLOTS, W]) for k in range(2)]
        win_be = [sb(f"win_be{k}", [P, SLOTS, W]) for k in range(2)]
        mid_hi = [sb(f"mid_hi{k}", [P, SLOTS, PADW], F32R) for k in range(2)]
        mid_lo = [sb(f"mid_lo{k}", [P, SLOTS, PADW], F32R) for k in range(2)]
        base_hl = [sb(f"base_hl{k}", [P, SLOTS, PADW], F32R) for k in range(2)]
        last_lh = [sb(f"last_lh{k}", [P, SLOTS, PADW], F32R) for k in range(2)]
        gate = sb("gate", [P, 2, 2, N])
        gated = sb("gated", [P, 2, 2, N])
        mixed = sb("mixed", [P, 2, 2, N])
        rows_out = sb("rows_out", [P, HALF, 2, W])

        w_nat = [sb(f"w_nat{k}", [C, C, TAPS, TAPS]) for k in range(2)]
        SECTIONS = ((BASE, MID), (0, BASE), (C - BASE, BASE))
        w_pad = [[sb(f"w_pad{k}_{t}", [C, TAPS, TAPS + 2, n]) for t, (c0, n) in enumerate(SECTIONS)]
                 for k in range(2)]
        w_hi = [[sb(f"w_hi{k}_{t}", [P, TAPS, P], F32R) for t in range(3)] for k in range(2)]
        w_lo = [[sb(f"w_lo{k}_{t}", [P, TAPS, P], F32R) for t in range(3)] for k in range(2)]
        ident = sb("ident", [C, C])
        prm_rows = sb("prm_rows", [10, P])
        prm = sb("prm", [P, 2, 5])
        veps = sb("veps", [P, 2])
        rvar = sb("rvar", [P, 2])
        rstd0 = sb("rstd0", [P, 2])
        sq = sb("sq", [P, 2])
        corr = sb("corr", [P, 2])
        rstd = sb("rstd", [P, 2])
        inv = sb("inv", [P, 2])
        mi = sb("mi", [P, 2])
        shift = sb("shift", [P, 2])
        gate_bias = sb("gate_bias", [P, 2])

        psum = ctx.enter_context(nc.psum_tensor("acc", [P, 8, BANK], F32))

        w_landed = [sem(f"w_landed{c}") for c in "ab"]
        prm_landed = sem("prm_landed")
        ident_ready = sem("ident_ready")
        wpad_ready = sem("wpad_ready")
        wt_ready = sem("wt_ready")
        whi_ready = sem("whi_ready")
        wlo_ready = sem("wlo_ready")
        prmdup_ready = sem("prmdup_ready")
        prmT_ready = sem("prmT_ready")
        rvar_ready = sem("rvar_ready")
        rstd0_ready = sem("rstd0_ready")
        prm_chain = sem("prm_chain")
        consts_ready = sem("consts_ready")
        edges_zero = sem("edges_zero")
        x_landed = sem("x_landed")
        win_landed = [sem(f"win_landed{c}") for c in "ab"]
        hi_ready = [sem(f"hi_ready{c}") for c in "ab"]
        lo_ready = [sem(f"lo_ready{c}") for c in "ab"]
        yp_ready = [sem(f"yp_ready{c}") for c in "ab"]
        yr_ready = [sem(f"yr_ready{c}") for c in "ab"]
        gate_ready = [sem(f"gate_ready{c}") for c in "ab"]
        gated_ready = [sem(f"gated_ready{c}") for c in "ab"]
        mixed_ready = [sem(f"mixed_ready{c}") for c in "ab"]
        resid_ready = sem("resid_ready")
        h_ready = sem("h_ready")
        out_ready = sem("out_ready")
        out_stored = [sem(f"out_stored{g}") for g in range(2)]

        def halves(i, g):
            return 2 * i + g + 1

        SPLITS = 3
        def splits(i, g, n=SPLITS):
            return 2 * SPLITS * i + SPLITS * g + n

        WIN_DMAS = 4 + 8
        def windows(i):
            return 16 * WIN_DMAS * (i + 1)

        def x_at(i):
            start = (i % RING) * (SLOTS * W)
            return x_pair[:, bass.ds(start, SLOTS * W)]

        def weight_parts(t):
            U, L = slice(P // 2, P), slice(0, P // 2)
            return ((slice(0, P), slice(0, P)),) if t == 0 else ((L, L), (U, L))

        def half_slots(g):
            return slice(g * HALF, (g + 1) * HALF)

        def banks(g, kind):
            b = 4 * g + 2 * kind
            return psum[:, b:b + 2, 0:N]

        FIRST, LAST = 0, B + 1

        def steps(eng, body):
            body(0)
            body(1)
            with eng.Fori(2, B - 2) as i:
                body(i, True)
            for i in range(B - 2, B + 2):
                body(i)

        def on(i, inner, low, high):
            return inner or low <= i < high

        block = ctx.enter_context(nc.Block())

        @block.sync
        def _(sp):
            x_rows = x.rearrange("b c (s q) w -> b q c s w", q=2)
            out_rows = out.rearrange("b c (g s) w -> b g c (s w)", g=2)

            def load_x(i):
                for q in range(2):
                    dst = x_at(i)[q * C:(q + 1) * C, :].rearrange("c (s w) -> c s w", w=W)
                    src = x_rows[bass.ds(i, 1), q].rearrange("b c s w -> (b c) s w")
                    sp.dma_start(dst, src).then_inc(x_landed, 16)

            def load_windows(src, k):
                parts = [(win_mid[k], 0, MID, BASE), (win_be[k], 0, BASE, 0),
                         (win_be[k], P // 2, BASE, C - BASE)]
                for r in range(4):
                    q = (r + 1) % 2
                    off = (r - 1 - q) // 2
                    lo, hi = max(0, -off), min(SLOTS, SLOTS - off)
                    for dst, p0, n, c0 in parts:
                        sp.dma_start(dst[p0 + r * n:p0 + (r + 1) * n, lo:hi, :]
                                     .rearrange("c s w -> c (s w)"),
                                     src[q * C + c0:q * C + c0 + n,
                                         (lo + off) * W:(hi + off) * W]).then_inc(win_landed[k], 16)

            def store(i, g):
                sp.wait_ge(out_ready, 2 * halves(i, g))
                dst = out_rows[bass.ds(i, 1), g].rearrange("b c n -> (b c) n")
                sp.dma_start(dst, rows_out[g * C:(g + 1) * C].rearrange("c s q w -> c (s q w)")
                             ).then_inc(out_stored[g], 16)

            for k, w in enumerate((w_a, w_b)):
                sp.dma_start(w_nat[k][:].rearrange("o i a b -> o (i a b)"),
                             w.rearrange("o i a b -> o (i a b)")).then_inc(w_landed[k], 16)
                if k == 0:
                    load_x(0)
            h_flat = h_pair[:].rearrange("p s w -> p (s w)")

            sp.wait_ge(edges_zero, 1)
            sp.wait_ge(x_landed, 32)
            load_windows(x_at(0), 0)
            load_x(1)

            def body(i, inner=False):
                if on(i, inner, 2, B + 2):
                    store(i - 2, 1)
                if on(i, inner, 0, B - 1):
                    sp.wait_ge(x_landed, 32 * (i + 2))
                    sp.wait_ge(lo_ready[0], splits(i, 1))
                    load_windows(x_at(i + 1), 0)
                if on(i, inner, 0, B - 2):
                    if on(i, inner, 2, B):
                        sp.wait_ge(resid_ready, halves(i - 2, 1))
                    load_x(i + 2)
                if on(i, inner, 0, B):
                    sp.wait_ge(h_ready, halves(i, 1))
                    if on(i, inner, 1, B):
                        sp.wait_ge(lo_ready[1], splits(i - 1, 1))
                    load_windows(h_flat, 1)
                if on(i, inner, 1, B + 1):
                    store(i - 1, 0)

            steps(sp, body)
            for g in range(2):
                sp.wait_ge(out_stored[g], 16 * B)

        @block.gpsimd
        def _(pool):
            rows = [theta_a, gamma_a, beta_a, mean_a, var_a, theta_b, gamma_b, beta_b, mean_b, var_b]
            for n, v in enumerate(rows):
                pool.dma_start(prm_rows[n:n + 1, 0:C], v.rearrange("(a c) -> a c", a=1)
                               ).then_inc(prm_landed, 16)
            nc.gpsimd.memset(ident[:], 0.0).then_inc(ident_ready, 1)
            pool.wait_ge(ident_ready, 1)
            nc.gpsimd.affine_select(out=ident[:], in_=ident[:], compare_op=ALU.not_equal, fill=1.0,
                                    base=0, pattern=[[-1, C]], channel_multiplier=1
                                    ).then_inc(ident_ready, 1)

        @block.tensor
        def _(pe):
            pe.wait_ge(ident_ready, 2)
            for k in range(2):
                for t, (c0, n) in enumerate(SECTIONS):
                    pe.wait_ge(wpad_ready, 2 * (3 * k + t + 1))
                    for dx in range(TAPS):
                        for q in range(2):
                            last = pe.transpose(
                                psum[0:4 * n, 3 * k + t, (2 * dx + q) * C:(2 * dx + q + 1) * C],
                                w_pad[k][t][:, dx, 1 - q:5 - q, :].rearrange("o r c -> o (r c)"),
                                ident[:])
                    last.then_inc(wt_ready, 1)
            pe.wait_ge(prmdup_ready, 1)
            pe.transpose(psum[:, 6, 0:10], prm_rows[:, :], ident[0:10, 0:10]).then_inc(prmT_ready, 1)
            pe.wait_ge(wlo_ready, 10)
            pe.wait_ge(rvar_ready, 1)

            def conv(k, i, g):
                yp = [(base_hl[k], w[k][1]) for w in (w_hi, w_lo)]
                yr = [(mid_hi[k], w_hi[k][0]), (mid_hi[k], w_lo[k][0]), (mid_lo[k], w_hi[k][0]),
                      (last_lh[k], w_hi[k][2]), (last_lh[k], w_lo[k][2])]
                pe.wait_ge(lo_ready[k], splits(i, g))
                for kind, pairs, done in ((0, yp, yp_ready[k]), (1, yr, yr_ready[k])):
                    units = [(m, w, dx) for m, w in pairs for dx in range(TAPS)]
                    for u, (m, w, dx) in enumerate(units):
                        for b in range(2):
                            s0 = g * HALF + b * BLK
                            last = pe.matmul(psum[:, 4 * g + 2 * kind + b, 0:N], w[:, dx, :],
                                             m[:, s0:s0 + BLK, dx:dx + W],
                                             start=(u == 0), stop=(u == len(units) - 1))
                    last.then_inc(done, 1)

            def body(i, inner=False):
                for g in range(2):
                    if on(i, inner, 0, B):
                        if on(i, inner, 2, B):
                            pe.wait_ge(mixed_ready[1], halves(i - 2, g))
                        conv(0, i, g)
                for g in range(2):
                    if on(i, inner, 1, B + 1):
                        if on(i, inner, 0, B):
                            pe.wait_ge(mixed_ready[0], halves(i, g))
                        else:
                            pe.wait_ge(mixed_ready[1], halves(i - 2, g))
                        conv(1, i - 1, g)

            steps(pe, body)

        @block.scalar
        def _(act):
            for n in range(6):
                act.wait_ge(wt_ready, n + 1)
                for dst, src in weight_parts(n % 3):
                    nc.scalar.activation(w_hi[n // 3][n % 3][dst].rearrange("p t m -> p (t m)"),
                                         psum[src, n, 0:TAPS * P], ACT.Copy).then_inc(whi_ready, 1)
            act.wait_ge(rvar_ready, 2)
            nc.scalar.activation(rstd0[:], rvar[:], ACT.Sqrt).then_inc(rstd0_ready, 1)

            def split_hi(k, i, g, inner):
                s = half_slots(g)
                if on(i, inner, 1, B):
                    act.wait_ge(yr_ready[k], halves(i - 1, g))
                if g == 0:
                    act.wait_ge(win_landed[k], windows(i))
                for dst, src in ((mid_hi[k][:], win_mid[k][:]),
                                 (base_hl[k][0:P // 2], win_be[k][0:P // 2]),
                                 (last_lh[k][P // 2:P], win_be[k][P // 2:P])):
                    nc.scalar.activation(dst[:, s, 1:1 + W], src[:, s, :], ACT.Copy
                                         ).then_inc(hi_ready[k], 1)

            def open_gate(k, i, g):
                act.wait_ge(yp_ready[k], halves(i, g))
                nc.scalar.activation(gate[:, g], banks(g, 0), ACT.Sigmoid, scale=ALPHA,
                                     bias=gate_bias[:, k:k + 1]).then_inc(gate_ready[k], 1)

            def norm_h(i, g, inner):
                act.wait_ge(mixed_ready[0], halves(i, g))
                if on(i, inner, 1, B):
                    act.wait_ge(win_landed[1], windows(i - 1))
                nc.scalar.activation(h_pair[:, half_slots(g), :].rearrange("p (b s) w -> p b (s w)", b=2),
                                     mixed[:, g], ACT.Relu, scale=inv[:, 0:1],
                                     bias=shift[:, 0:1]).then_inc(h_ready, 1)

            def finish(i, g, inner):
                act.wait_ge(resid_ready, halves(i, g))
                if on(i, inner, 1, B):
                    act.wait_ge(out_stored[g], 16 * i)
                for q in range(2):
                    nc.scalar.activation(
                        rows_out[g * C:(g + 1) * C, :, q, :],
                        gated[q * C:(q + 1) * C, g].rearrange("c b (s w) -> c (b s) w", w=W),
                        ACT.Relu, bias=shift[q * C:(q + 1) * C, 1:2]).then_inc(out_ready, 1)

            act.wait_ge(edges_zero, 1)
            split_hi(0, 0, 0, False)
            split_hi(0, 0, 1, False)
            act.wait_ge(consts_ready, 1)

            def body(i, inner=False):
                if on(i, inner, 0, B):
                    open_gate(0, i, 0)
                if on(i, inner, 2, B + 2):
                    finish(i - 2, 1, inner)
                for g in range(2):
                    if on(i, inner, 1, B + 1):
                        split_hi(1, i - 1, g, inner)
                if on(i, inner, 0, B):
                    norm_h(i, 0, inner)
                    open_gate(0, i, 1)
                if on(i, inner, 0, B - 1):
                    split_hi(0, i + 1, 0, inner)
                if on(i, inner, 0, B):
                    norm_h(i, 1, inner)
                if on(i, inner, 1, B + 1):
                    open_gate(1, i - 1, 0)
                if on(i, inner, 0, B - 1):
                    split_hi(0, i + 1, 1, inner)
                if on(i, inner, 1, B + 1):
                    open_gate(1, i - 1, 1)
                    finish(i - 1, 0, inner)

            steps(act, body)

        @block.vector
        def _(dve):
            for k in range(2):
                for t in (win_mid[k], win_be[k]):
                    for s in (0, SLOTS - 1):
                        nc.vector.memset(t[:, s, :], 0.0)
                for t in (mid_hi[k], mid_lo[k], base_hl[k], last_lh[k]):
                    last = nc.vector.memset(t[:, :, 0:PADW:PADW - 1].bitcast(F32), 0.0)
            last.then_inc(edges_zero, 1)
            for k in range(2):
                dve.wait_ge(w_landed[k], 16)
                for t, (c0, n) in enumerate(SECTIONS):
                    nc.vector.memset(w_pad[k][t][:, :, 0:5:4, :], 0.0).then_inc(wpad_ready, 1)
                    nc.vector.tensor_copy(w_pad[k][t][:, :, 1:4, :],
                                          w_nat[k][:, c0:c0 + n].rearrange("o i a b -> o b a i")
                                          ).then_inc(wpad_ready, 1)
            dve.wait_ge(prm_landed, 160)
            nc.vector.tensor_copy(prm_rows[:, C:P], prm_rows[:, 0:C]).then_inc(prmdup_ready, 1)

            chain = [0]

            def link(ins):
                chain[0] += 1
                ins.then_inc(prm_chain, 1)
                dve.wait_ge(prm_chain, chain[0])

            dve.wait_ge(prmT_ready, 1)
            nc.vector.tensor_copy(prm[:].rearrange("p k n -> p (k n)"), psum[:, 6, 0:10]
                                  ).then_inc(rvar_ready, 1)
            dve.wait_ge(rvar_ready, 1)
            theta, gamma, beta, mean, var = (prm[:, :, n] for n in range(5))
            link(nc.vector.tensor_scalar(veps[:], var, EPS, None, ALU.add))
            nc.vector.reciprocal(rvar[:], veps[:]).then_inc(rvar_ready, 1)
            made = 0
            for n in range(6):
                made += len(weight_parts(n % 3))
                dve.wait_ge(whi_ready, made)
                for dst, src in weight_parts(n % 3):
                    hi = w_hi[n // 3][n % 3][dst].rearrange("p t m -> p (t m)")
                    nc.vector.tensor_tensor(w_lo[n // 3][n % 3][dst].rearrange("p t m -> p (t m)"),
                                            psum[src, n, 0:TAPS * P], hi.bitcast(F32), ALU.subtract
                                            ).then_inc(wlo_ready, 1)
            dve.wait_ge(rstd0_ready, 1)
            link(nc.vector.tensor_tensor(sq[:], rstd0[:], rstd0[:], ALU.mult))
            link(nc.vector.tensor_tensor(corr[:], sq[:], veps[:], ALU.mult))
            link(nc.vector.tensor_scalar(corr[:], corr[:], -0.5, 1.5, ALU.mult, ALU.add))
            link(nc.vector.tensor_tensor(rstd[:], rstd0[:], corr[:], ALU.mult))
            link(nc.vector.tensor_tensor(inv[:], gamma, rstd[:], ALU.mult))
            link(nc.vector.tensor_tensor(mi[:], mean, inv[:], ALU.mult))
            link(nc.vector.tensor_tensor(shift[:], beta, mi[:], ALU.subtract))
            nc.vector.tensor_scalar(gate_bias[:], theta, -ALPHA, None, ALU.mult
                                    ).then_inc(consts_ready, 1)

            def split_lo(k, i, g):
                s = half_slots(g)
                mid, be = win_mid[k], win_be[k]
                U, L = slice(P // 2, P), slice(0, P // 2)
                for n, (dst, src, hi) in enumerate((
                        (mid_lo[k][:], mid[:], mid_hi[k][:]),
                        (base_hl[k][U], be[L], base_hl[k][L]),
                        (last_lh[k][L], be[U], last_lh[k][U]))):
                    dve.wait_ge(hi_ready[k], splits(i, g, n + 1))
                    nc.vector.tensor_tensor(dst[:, s, 1:1 + W], src[:, s, :],
                                            hi[:, s, 1:1 + W].bitcast(F32), ALU.subtract
                                            ).then_inc(lo_ready[k], 1)

            def mix(k, i, g, inner):
                dve.wait_ge(gate_ready[k], halves(i, g))
                dve.wait_ge(yr_ready[k], halves(i, g))
                if k == 0:
                    if on(i, inner, 2, B):
                        dve.wait_ge(out_ready, 2 * halves(i - 2, g))
                else:
                    if on(i, False, B - 1, B) and not inner:
                        dve.wait_ge(out_ready, 2 * halves(i - 1, g))
                nc.vector.tensor_tensor(gated[:, g], gate[:, g], banks(g, 1), ALU.mult
                                        ).then_inc(gated_ready[k], 1)
                dve.wait_ge(gated_ready[k], halves(i, g))
                if k == 1:
                    dve.wait_ge(h_ready, halves(i + 1, g) if (inner or i + 1 < B) else 2 * B)
                nc.vector.tensor_tensor(mixed[:, g], gated[:, g], banks(g, 0), ALU.add
                                        ).then_inc(mixed_ready[k], 1)
                if k == 1:
                    dve.wait_ge(mixed_ready[1], halves(i, g))
                    xs = x_at(i).rearrange("p (g b n) -> p g b n", g=2, b=2)[:, g]
                    nc.vector.scalar_tensor_tensor(gated[:, g], mixed[:, g], inv[:, 1:2], xs,
                                                   ALU.mult, ALU.add).then_inc(resid_ready, 1)

            dve.wait_ge(edges_zero, 1)
            for g in range(2):
                split_lo(0, 0, g)

            def body(i, inner=False):
                if on(i, inner, 2, B + 2):
                    mix(1, i - 2, 1, inner)
                for g in range(2):
                    if on(i, inner, 1, B + 1):
                        split_lo(1, i - 1, g)
                for g in range(2):
                    if on(i, inner, 0, B):
                        mix(0, i, g, inner)
                    if on(i, inner, 0, B - 1):
                        split_lo(0, i + 1, g)
                if on(i, inner, 1, B + 1):
                    mix(1, i - 1, 0, inner)

            steps(dve, body)


_PARAMS = [f"L0_conv_{n}_{c}" for c in "ab" for n in ("w", "theta", "gamma", "beta", "mean", "var")]
_INS = ["x"] + _PARAMS


def kernel(**inputs):
    import numpy as _np
    import concourse.bacc as _bacc
    from concourse import mybir as _mybir
    from concourse.bass_utils import run_bass_kernel_spmd as _run

    nc = _bacc.Bacc("TRN2", target_bir_lowering=False, num_devices=1)
    arrays, args = {}, []
    for name in _INS:
        a = _np.ascontiguousarray(inputs[name])
        arrays[f"in_{name}_dram"] = a
        args.append(nc.dram_tensor(f"in_{name}_dram", a.shape, _mybir.dt.from_np(a.dtype), kind="ExternalInput").ap())
    shape = inputs["x"].shape
    args.append(nc.dram_tensor("out_0_dram", shape, _mybir.dt.from_np(_np.dtype("float32")), kind="ExternalOutput").ap())
    gated_conv_pair_kernel(nc, *args)
    r = _run(nc, [arrays], core_ids=[0])
    return r.results[0]["out_0_dram"]
```

```python
from contextlib import ExitStack

import concourse.bass as bass
from concourse import mybir

ALU = mybir.AluOpType
ACT = mybir.ActivationFunctionType
F32 = mybir.dt.float32
F32R = mybir.dt.float32r

P = 128
EPS = 1e-5
ALPHA = 2.0
GROUPS = 4
TAPS = 3
RING = 4
BANK = 512


def gated_conv_pair_kernel(nc, x, w_a, theta_a, gamma_a, beta_a, mean_a, var_a,
                           w_b, theta_b, gamma_b, beta_b, mean_b, var_b, out):
    B, C, H, W = x.shape
    assert 2 * C == P and H % 8 == 0
    BASE = C // GROUPS
    MID = 2 * BASE
    SLOTS = H // 2
    HALF = SLOTS // 2
    BLK = HALF // 2
    N = BLK * W
    PADW = W + 2
    assert N <= BANK and 4 * MID == P and 8 * BASE == P

    with ExitStack() as ctx:
        def sb(name, shape, dt=F32):
            return ctx.enter_context(nc.sbuf_tensor(name, shape, dt))

        def sem(name):
            return ctx.enter_context(nc.semaphore(name))

        x_pair = sb("x_pair", [P, RING * SLOTS * W])
        h_pair = sb("h_pair", [P, SLOTS, W])
        win_mid = [sb(f"win_mid{k}", [P, SLOTS, W]) for k in range(2)]
        win_be = [sb(f"win_be{k}", [P, SLOTS, W]) for k in range(2)]
        mid_hi = [sb(f"mid_hi{k}", [P, SLOTS, PADW], F32R) for k in range(2)]
        mid_lo = [sb(f"mid_lo{k}", [P, SLOTS, PADW], F32R) for k in range(2)]
        base_hl = [sb(f"base_hl{k}", [P, SLOTS, PADW], F32R) for k in range(2)]
        last_lh = [sb(f"last_lh{k}", [P, SLOTS, PADW], F32R) for k in range(2)]
        base_hh = [sb(f"base_hh{k}", [P, SLOTS, PADW], F32R) for k in range(2)]
        last_hh = [sb(f"last_hh{k}", [P, SLOTS, PADW], F32R) for k in range(2)]
        gate = sb("gate", [P, 2, 2, N])
        gated = sb("gated", [P, 2, 2, N])
        mixed = sb("mixed", [P, 2, 2, N])
        rows_out = sb("rows_out", [P, HALF, 2, W])

        w_nat = [sb(f"w_nat{k}", [C, C, TAPS, TAPS]) for k in range(2)]
        SECTIONS = ((BASE, MID), (0, BASE), (C - BASE, BASE))
        w_pad = [[sb(f"w_pad{k}_{t}", [C, TAPS, TAPS + 2, n]) for t, (c0, n) in enumerate(SECTIONS)]
                 for k in range(2)]
        w_hi = [[sb(f"w_hi{k}_{t}", [P, TAPS, P], F32R) for t in range(3)] for k in range(2)]
        w_lo = [[sb(f"w_lo{k}_{t}", [P, TAPS, P], F32R) for t in range(3)] for k in range(2)]
        w_two = [[sb(f"w_two{k}_{t}", [P, P], F32R) for t in range(1, 3)] for k in range(2)]
        ident = sb("ident", [C, C])
        prm_rows = sb("prm_rows", [10, P])
        prm = sb("prm", [P, 2, 5])
        veps = sb("veps", [P, 2])
        rvar = sb("rvar", [P, 2])
        rstd0 = sb("rstd0", [P, 2])
        sq = sb("sq", [P, 2])
        corr = sb("corr", [P, 2])
        rstd = sb("rstd", [P, 2])
        inv = sb("inv", [P, 2])
        mi = sb("mi", [P, 2])
        shift = sb("shift", [P, 2])
        gate_bias = sb("gate_bias", [P, 2])

        psum = ctx.enter_context(nc.psum_tensor("acc", [P, 8, BANK], F32))

        w_landed = [sem(f"w_landed{c}") for c in "ab"]
        prm_landed = sem("prm_landed")
        ident_ready = sem("ident_ready")
        wpad_ready = sem("wpad_ready")
        wt_ready = sem("wt_ready")
        whi_ready = sem("whi_ready")
        wlo_ready = sem("wlo_ready")
        prmdup_ready = sem("prmdup_ready")
        prmT_ready = sem("prmT_ready")
        rvar_ready = sem("rvar_ready")
        rstd0_ready = sem("rstd0_ready")
        prm_chain = sem("prm_chain")
        consts_ready = sem("consts_ready")
        edges_zero = sem("edges_zero")
        x_landed = sem("x_landed")
        mid_landed = [sem(f"mid_landed{c}") for c in "ab"]
        be_landed = [sem(f"be_landed{c}") for c in "ab"]
        hi_ready = [sem(f"hi_ready{c}") for c in "ab"]
        lo_ready = [sem(f"lo_ready{c}") for c in "ab"]
        hh_landed = [[sem(f"hh_landed{c}{g}") for g in range(2)] for c in "ab"]
        spread_started = sem("spread_started")
        wtwo_ready = sem("wtwo_ready")
        yp_ready = [sem(f"yp_ready{c}") for c in "ab"]
        yr_ready = [sem(f"yr_ready{c}") for c in "ab"]
        gate_ready = [sem(f"gate_ready{c}") for c in "ab"]
        gated_ready = [sem(f"gated_ready{c}") for c in "ab"]
        mixed_ready = [sem(f"mixed_ready{c}") for c in "ab"]
        resid_ready = sem("resid_ready")
        h_ready = sem("h_ready")
        out_ready = sem("out_ready")
        out_stored = [sem(f"out_stored{g}") for g in range(2)]

        def halves(i, g):
            return 2 * i + g + 1

        SPLITS = 4
        def splits(i, g, n=SPLITS):
            return 2 * SPLITS * i + SPLITS * g + n

        def windows(i, dmas):
            return 16 * dmas * (i + 1)

        def x_at(i):
            start = (i % RING) * (SLOTS * W)
            return x_pair[:, bass.ds(start, SLOTS * W)]

        def weight_parts(t):
            U, L = slice(P // 2, P), slice(0, P // 2)
            return ((slice(0, P), slice(0, P)),) if t == 0 else ((L, L), (U, L))

        def half_slots(g):
            return slice(g * HALF, (g + 1) * HALF)

        def banks(g, kind):
            b = 4 * g + 2 * kind
            return psum[:, b:b + 2, 0:N]

        FIRST, LAST = 0, B + 1

        def steps(eng, body):
            body(0)
            body(1)
            with eng.Fori(2, B - 2) as i:
                body(i, True)
            for i in range(B - 2, B + 2):
                body(i)

        def on(i, inner, low, high):
            return inner or low <= i < high

        block = ctx.enter_context(nc.Block())

        @block.sync
        def _(sp):
            x_rows = x.rearrange("b c (s q) w -> b q c s w", q=2)
            out_rows = out.rearrange("b c (g s) w -> b g c (s w)", g=2)

            def load_x(i):
                for q in range(2):
                    dst = x_at(i)[q * C:(q + 1) * C, :].rearrange("c (s w) -> c s w", w=W)
                    src = x_rows[bass.ds(i, 1), q].rearrange("b c s w -> (b c) s w")
                    sp.dma_start(dst, src).then_inc(x_landed, 16)

            def load_windows(src, k):
                for dst, p0, n, c0, landed in ((win_mid[k], 0, MID, BASE, mid_landed[k]),
                                               (win_be[k], 0, BASE, 0, be_landed[k]),
                                               (win_be[k], P // 2, BASE, C - BASE, be_landed[k])):
                    for r in range(4):
                        q = (r + 1) % 2
                        off = (r - 1 - q) // 2
                        lo, hi = max(0, -off), min(SLOTS, SLOTS - off)
                        sp.dma_start(dst[p0 + r * n:p0 + (r + 1) * n, lo:hi, :]
                                     .rearrange("c s w -> c (s w)"),
                                     src[q * C + c0:q * C + c0 + n,
                                         (lo + off) * W:(hi + off) * W]).then_inc(landed, 16)

            def store(i, g):
                sp.wait_ge(out_ready, 2 * halves(i, g))
                dst = out_rows[bass.ds(i, 1), g].rearrange("b c n -> (b c) n")
                sp.dma_start(dst, rows_out[g * C:(g + 1) * C].rearrange("c s q w -> c (s q w)")
                             ).then_inc(out_stored[g], 16)

            for k, w in enumerate((w_a, w_b)):
                sp.dma_start(w_nat[k][:].rearrange("o i a b -> o (i a b)"),
                             w.rearrange("o i a b -> o (i a b)")).then_inc(w_landed[k], 16)
                if k == 0:
                    load_x(0)
            h_flat = h_pair[:].rearrange("p s w -> p (s w)")

            sp.wait_ge(edges_zero, 1)
            sp.wait_ge(x_landed, 32)
            load_windows(x_at(0), 0)
            load_x(1)

            def body(i, inner=False):
                if on(i, inner, 0, B - 1):
                    sp.wait_ge(x_landed, 32 * (i + 2))
                    sp.wait_ge(hi_ready[0], splits(i, 1))
                    sp.wait_ge(lo_ready[0], splits(i, 1))
                    load_windows(x_at(i + 1), 0)
                if on(i, inner, 2, B + 2):
                    store(i - 2, 1)
                if on(i, inner, 0, B - 2):
                    if on(i, inner, 2, B):
                        sp.wait_ge(resid_ready, halves(i - 2, 1))
                    load_x(i + 2)
                if on(i, inner, 0, B):
                    sp.wait_ge(h_ready, halves(i, 1))
                    if on(i, inner, 1, B):
                        sp.wait_ge(hi_ready[1], splits(i - 1, 1))
                        sp.wait_ge(lo_ready[1], splits(i - 1, 1))
                    load_windows(h_flat, 1)
                if on(i, inner, 1, B + 1):
                    store(i - 1, 0)

            steps(sp, body)
            for g in range(2):
                sp.wait_ge(out_stored[g], 16 * B)

        @block.gpsimd
        def _(pool):
            rows = [theta_a, gamma_a, beta_a, mean_a, var_a, theta_b, gamma_b, beta_b, mean_b, var_b]
            for n, v in enumerate(rows):
                pool.dma_start(prm_rows[n:n + 1, 0:C], v.rearrange("(a c) -> a c", a=1)
                               ).then_inc(prm_landed, 16)
            nc.gpsimd.memset(ident[:], 0.0).then_inc(ident_ready, 1)
            pool.wait_ge(ident_ready, 1)
            nc.gpsimd.affine_select(out=ident[:], in_=ident[:], compare_op=ALU.not_equal, fill=1.0,
                                    base=0, pattern=[[-1, C]], channel_multiplier=1
                                    ).then_inc(ident_ready, 1)

            def spread(k, i):
                flat_from = last_lh[k][P // 2:P].rearrange("p s w -> p (s w)").bitcast(F32)
                flat_to = last_hh[k][:].rearrange("p s w -> p (s w)").bitcast(F32)
                for g in range(2):
                    a, z = g * HALF * PADW, (g + 1) * HALF * PADW
                    pool.wait_ge(hi_ready[k], splits(i, g, 3))
                    pool.sem_inc(spread_started, 1)
                    for half in range(2):
                        pool.dma_start(flat_to[half * (P // 2):(half + 1) * (P // 2), a:z - 1],
                                       flat_from[:, a + half:z - 1 + half]
                                       ).then_inc(hh_landed[k][g], 16)

            pool.wait_ge(edges_zero, 1)
            spread(0, 0)

            def body(i, inner=False):
                if on(i, inner, 1, B + 1):
                    spread(1, i - 1)
                if on(i, inner, 0, B - 1):
                    spread(0, i + 1)

            steps(pool, body)

        @block.tensor
        def _(pe):
            pe.wait_ge(ident_ready, 2)
            for k in range(2):
                for t, (c0, n) in enumerate(SECTIONS):
                    pe.wait_ge(wpad_ready, 2 * (3 * k + t + 1))
                    for dx in range(TAPS):
                        for q in range(2):
                            last = pe.transpose(
                                psum[0:4 * n, 3 * k + t, (2 * dx + q) * C:(2 * dx + q + 1) * C],
                                w_pad[k][t][:, dx, 1 - q:5 - q, :].rearrange("o r c -> o (r c)"),
                                ident[:])
                    last.then_inc(wt_ready, 1)
            pe.wait_ge(prmdup_ready, 1)
            pe.transpose(psum[:, 6, 0:10], prm_rows[:, :], ident[0:10, 0:10]).then_inc(prmT_ready, 1)
            pe.wait_ge(wtwo_ready, 8)
            pe.wait_ge(rvar_ready, 1)

            def conv(k, i, g):
                taps = range(TAPS)
                mid_h, mid_l, base, last = mid_hi[k], mid_lo[k], base_hl[k], last_lh[k]
                yp = [(base, w_hi[k][1][:, dx], dx) for dx in taps]
                yp += [(base, w_lo[k][1][:, 2], 2), (base_hh[k], w_two[k][0][:], 0)]
                yr = [(mid_h, w_hi[k][0][:, dx], dx) for dx in taps]
                yr += [(mid_h, w_lo[k][0][:, dx], dx) for dx in taps]
                yr += [(mid_l, w_hi[k][0][:, dx], dx) for dx in taps]
                yr += [(last, w_hi[k][2][:, dx], dx) for dx in taps]
                yr += [(last, w_lo[k][2][:, 2], 2), (last_hh[k], w_two[k][1][:], 0)]
                pe.wait_ge(hi_ready[k], splits(i, g))
                pe.wait_ge(lo_ready[k], splits(i, g))
                for kind, units, done in ((0, yp, yp_ready[k]), (1, yr, yr_ready[k])):
                    for u, (m, w, dx) in enumerate(units):
                        if m is last_hh[k]:
                            pe.wait_ge(hh_landed[k][g], 32 * (i + 1))
                        for b in range(2):
                            s0 = g * HALF + b * BLK
                            mm = pe.matmul(psum[:, 4 * g + 2 * kind + b, 0:N], w,
                                           m[:, s0:s0 + BLK, dx:dx + W],
                                           start=(u == 0), stop=(u == len(units) - 1))
                    mm.then_inc(done, 1)

            def body(i, inner=False):
                for g in range(2):
                    if on(i, inner, 0, B):
                        if on(i, inner, 2, B):
                            pe.wait_ge(mixed_ready[1], halves(i - 2, g))
                        conv(0, i, g)
                for g in range(2):
                    if on(i, inner, 1, B + 1):
                        if on(i, inner, 0, B):
                            pe.wait_ge(mixed_ready[0], halves(i, g))
                        else:
                            pe.wait_ge(mixed_ready[1], halves(i - 2, g))
                        conv(1, i - 1, g)

            steps(pe, body)

        @block.scalar
        def _(act):
            for n in range(6):
                act.wait_ge(wt_ready, n + 1)
                for dst, src in weight_parts(n % 3):
                    nc.scalar.activation(w_hi[n // 3][n % 3][dst].rearrange("p t m -> p (t m)"),
                                         psum[src, n, 0:TAPS * P], ACT.Copy).then_inc(whi_ready, 1)
            act.wait_ge(rvar_ready, 2)
            nc.scalar.activation(rstd0[:], rvar[:], ACT.Sqrt).then_inc(rstd0_ready, 1)

            def split_hi(k, i, g, inner, parts=range(SPLITS)):
                s = half_slots(g)
                U, L = slice(P // 2, P), slice(0, P // 2)
                if 0 in parts and on(i, inner, 1, B):
                    act.wait_ge(yr_ready[k], halves(i - 1, g))
                for n in parts:
                    if g == 0 and n == 0:
                        act.wait_ge(mid_landed[k], windows(i, 4))
                    if g == 0 and n == 1:
                        act.wait_ge(be_landed[k], windows(i, 8))
                    dst, src = ((mid_hi[k][:], win_mid[k][:]), (base_hl[k][L], win_be[k][L]),
                                (last_lh[k][U], win_be[k][U]), (base_hh[k][L], win_be[k][L]))[n]
                    nc.scalar.activation(dst[:, s, 1:1 + W], src[:, s, :], ACT.Copy
                                         ).then_inc(hi_ready[k], 1)

            def open_gate(k, i, g):
                act.wait_ge(yp_ready[k], halves(i, g))
                nc.scalar.activation(gate[:, g], banks(g, 0), ACT.Sigmoid, scale=ALPHA,
                                     bias=gate_bias[:, k:k + 1]).then_inc(gate_ready[k], 1)

            def norm_h(i, g, inner):
                act.wait_ge(mixed_ready[0], halves(i, g))
                if on(i, inner, 1, B):
                    act.wait_ge(mid_landed[1], windows(i - 1, 4))
                    act.wait_ge(be_landed[1], windows(i - 1, 8))
                nc.scalar.activation(h_pair[:, half_slots(g), :].rearrange("p (b s) w -> p b (s w)", b=2),
                                     mixed[:, g], ACT.Relu, scale=inv[:, 0:1],
                                     bias=shift[:, 0:1]).then_inc(h_ready, 1)

            def finish(i, g, inner):
                act.wait_ge(resid_ready, halves(i, g))
                if on(i, inner, 1, B):
                    act.wait_ge(out_stored[g], 16 * i)
                for q in range(2):
                    nc.scalar.activation(
                        rows_out[g * C:(g + 1) * C, :, q, :],
                        gated[q * C:(q + 1) * C, g].rearrange("c b (s w) -> c (b s) w", w=W),
                        ACT.Relu, bias=shift[q * C:(q + 1) * C, 1:2]).then_inc(out_ready, 1)

            act.wait_ge(edges_zero, 1)
            split_hi(0, 0, 0, False)
            split_hi(0, 0, 1, False)
            act.wait_ge(consts_ready, 1)

            def body(i, inner=False):
                a, b, after = on(i, inner, 0, B), on(i, inner, 1, B + 1), on(i, inner, 0, B - 1)
                before = on(i, inner, 2, B + 2)
                for g in range(2):
                    if b:
                        split_hi(1, i - 1, g, inner, range(3))
                    if a:
                        open_gate(0, i, g)
                    if g == 0 and before:
                        finish(i - 2, 1, inner)
                    if g == 1 and a:
                        norm_h(i, 0, inner)
                    if b:
                        split_hi(1, i - 1, g, inner, [3])
                for g in range(2):
                    if after:
                        split_hi(0, i + 1, g, inner, range(3))
                    if b:
                        open_gate(1, i - 1, g)
                    if g == 0 and a:
                        norm_h(i, 1, inner)
                    if g == 1 and b:
                        finish(i - 1, 0, inner)
                    if after:
                        split_hi(0, i + 1, g, inner, [3])

            steps(act, body)

        @block.vector
        def _(dve):
            for k in range(2):
                for t in (win_mid[k], win_be[k]):
                    for s in (0, SLOTS - 1):
                        nc.vector.memset(t[:, s, :], 0.0)
                for t in (mid_hi[k], mid_lo[k], base_hl[k], last_lh[k], base_hh[k]):
                    last = nc.vector.memset(t[:, :, 0:PADW:PADW - 1].bitcast(F32), 0.0)
            last.then_inc(edges_zero, 1)
            for k in range(2):
                dve.wait_ge(w_landed[k], 16)
                for t, (c0, n) in enumerate(SECTIONS):
                    nc.vector.memset(w_pad[k][t][:, :, 0:5:4, :], 0.0).then_inc(wpad_ready, 1)
                    nc.vector.tensor_copy(w_pad[k][t][:, :, 1:4, :],
                                          w_nat[k][:, c0:c0 + n].rearrange("o i a b -> o b a i")
                                          ).then_inc(wpad_ready, 1)
            dve.wait_ge(prm_landed, 160)
            nc.vector.tensor_copy(prm_rows[:, C:P], prm_rows[:, 0:C]).then_inc(prmdup_ready, 1)

            chain = [0]

            def link(ins):
                chain[0] += 1
                ins.then_inc(prm_chain, 1)
                dve.wait_ge(prm_chain, chain[0])

            dve.wait_ge(prmT_ready, 1)
            nc.vector.tensor_copy(prm[:].rearrange("p k n -> p (k n)"), psum[:, 6, 0:10]
                                  ).then_inc(rvar_ready, 1)
            dve.wait_ge(rvar_ready, 1)
            theta, gamma, beta, mean, var = (prm[:, :, n] for n in range(5))
            link(nc.vector.tensor_scalar(veps[:], var, EPS, None, ALU.add))
            nc.vector.reciprocal(rvar[:], veps[:]).then_inc(rvar_ready, 1)
            made = 0
            for n in range(6):
                made += len(weight_parts(n % 3))
                dve.wait_ge(whi_ready, made)
                for dst, src in weight_parts(n % 3):
                    hi = w_hi[n // 3][n % 3][dst].rearrange("p t m -> p (t m)")
                    nc.vector.tensor_tensor(w_lo[n // 3][n % 3][dst].rearrange("p t m -> p (t m)"),
                                            psum[src, n, 0:TAPS * P], hi.bitcast(F32), ALU.subtract
                                            ).then_inc(wlo_ready, 1)
            dve.wait_ge(wlo_ready, made)
            for k in range(2):
                for t in range(1, 3):
                    for h in range(2):
                        part = slice(h * (P // 2), (h + 1) * (P // 2))
                        nc.vector.tensor_copy(w_two[k][t - 1][part], w_lo[k][t][part, h].bitcast(F32)
                                              ).then_inc(wtwo_ready, 1)
            dve.wait_ge(rstd0_ready, 1)
            link(nc.vector.tensor_tensor(sq[:], rstd0[:], rstd0[:], ALU.mult))
            link(nc.vector.tensor_tensor(corr[:], sq[:], veps[:], ALU.mult))
            link(nc.vector.tensor_scalar(corr[:], corr[:], -0.5, 1.5, ALU.mult, ALU.add))
            link(nc.vector.tensor_tensor(rstd[:], rstd0[:], corr[:], ALU.mult))
            link(nc.vector.tensor_tensor(inv[:], gamma, rstd[:], ALU.mult))
            link(nc.vector.tensor_tensor(mi[:], mean, inv[:], ALU.mult))
            link(nc.vector.tensor_tensor(shift[:], beta, mi[:], ALU.subtract))
            nc.vector.tensor_scalar(gate_bias[:], theta, -ALPHA, None, ALU.mult
                                    ).then_inc(consts_ready, 1)

            def split_lo(k, i, g):
                s = half_slots(g)
                mid, be = win_mid[k], win_be[k]
                U, L = slice(P // 2, P), slice(0, P // 2)
                for n, (dst, src, hi) in ((1, (mid_lo[k][:], mid[:], mid_hi[k][:])),
                                          (2, (base_hl[k][U], be[L], base_hl[k][L])),
                                          (3, (last_lh[k][L], be[U], last_lh[k][U]))):
                    dve.wait_ge(hi_ready[k], splits(i, g, n))
                    nc.vector.tensor_tensor(dst[:, s, 1:1 + W], src[:, s, :],
                                            hi[:, s, 1:1 + W].bitcast(F32), ALU.subtract
                                            ).then_inc(lo_ready[k], 1)
                nc.vector.tensor_copy(base_hh[k][U, s, 0:W], be[L, s, :]).then_inc(lo_ready[k], 1)

            def mix(k, i, g, inner):
                dve.wait_ge(gate_ready[k], halves(i, g))
                dve.wait_ge(yr_ready[k], halves(i, g))
                if k == 0:
                    if on(i, inner, 2, B):
                        dve.wait_ge(out_ready, 2 * halves(i - 2, g))
                else:
                    if on(i, False, B - 1, B) and not inner:
                        dve.wait_ge(out_ready, 2 * halves(i - 1, g))
                nc.vector.tensor_tensor(gated[:, g], gate[:, g], banks(g, 1), ALU.mult
                                        ).then_inc(gated_ready[k], 1)
                dve.wait_ge(gated_ready[k], halves(i, g))
                if k == 1:
                    dve.wait_ge(h_ready, halves(i + 1, g) if (inner or i + 1 < B) else 2 * B)
                nc.vector.tensor_tensor(mixed[:, g], gated[:, g], banks(g, 0), ALU.add
                                        ).then_inc(mixed_ready[k], 1)
                if k == 1:
                    dve.wait_ge(mixed_ready[1], halves(i, g))
                    xs = x_at(i).rearrange("p (g b n) -> p g b n", g=2, b=2)[:, g]
                    nc.vector.scalar_tensor_tensor(gated[:, g], mixed[:, g], inv[:, 1:2], xs,
                                                   ALU.mult, ALU.add).then_inc(resid_ready, 1)

            dve.wait_ge(edges_zero, 1)
            for g in range(2):
                split_lo(0, 0, g)

            def body(i, inner=False):
                a, b, after = on(i, inner, 0, B), on(i, inner, 1, B + 1), on(i, inner, 0, B - 1)
                if on(i, inner, 2, B + 2):
                    mix(1, i - 2, 1, inner)
                if b:
                    split_lo(1, i - 1, 0)
                if a:
                    mix(0, i, 0, inner)
                if b:
                    split_lo(1, i - 1, 1)
                if a:
                    mix(0, i, 1, inner)
                if after:
                    split_lo(0, i + 1, 0)
                if b:
                    mix(1, i - 1, 0, inner)
                if after:
                    split_lo(0, i + 1, 1)

            steps(dve, body)


_PARAMS = [f"L0_conv_{n}_{c}" for c in "ab" for n in ("w", "theta", "gamma", "beta", "mean", "var")]
_INS = ["x"] + _PARAMS


def kernel(**inputs):
    import numpy as _np
    import concourse.bacc as _bacc
    from concourse import mybir as _mybir
    from concourse.bass_utils import run_bass_kernel_spmd as _run

    nc = _bacc.Bacc("TRN2", target_bir_lowering=False, num_devices=1)
    arrays, args = {}, []
    for name in _INS:
        a = _np.ascontiguousarray(inputs[name])
        arrays[f"in_{name}_dram"] = a
        args.append(nc.dram_tensor(f"in_{name}_dram", a.shape, _mybir.dt.from_np(a.dtype), kind="ExternalInput").ap())
    shape = inputs["x"].shape
    args.append(nc.dram_tensor("out_0_dram", shape, _mybir.dt.from_np(_np.dtype("float32")), kind="ExternalOutput").ap())
    gated_conv_pair_kernel(nc, *args)
    r = _run(nc, [arrays], core_ids=[0])
    return r.results[0]["out_0_dram"]
```

```python
from contextlib import ExitStack

import concourse.bass as bass
from concourse import mybir

ALU = mybir.AluOpType
ACT = mybir.ActivationFunctionType
F32 = mybir.dt.float32
F32R = mybir.dt.float32r

P = 128
EPS = 1e-5
ALPHA = 2.0
GROUPS = 4
TAPS = 3
RING = 4
BANK = 512


def gated_conv_pair_kernel(nc, x, w_a, theta_a, gamma_a, beta_a, mean_a, var_a,
                           w_b, theta_b, gamma_b, beta_b, mean_b, var_b, out):
    B, C, H, W = x.shape
    assert 2 * C == P and H % 8 == 0
    BASE = C // GROUPS
    MID = 2 * BASE
    SLOTS = H // 2
    HALF = SLOTS // 2
    BLK = HALF // 2
    N = BLK * W
    PADW = W + 2
    assert N <= BANK and 4 * MID == P and 8 * BASE == P

    with ExitStack() as ctx:
        def sb(name, shape, dt=F32):
            return ctx.enter_context(nc.sbuf_tensor(name, shape, dt))

        def sem(name):
            return ctx.enter_context(nc.semaphore(name))

        x_pair = sb("x_pair", [P, RING * SLOTS * W])
        h_pair = sb("h_pair", [P, SLOTS, W])
        win_mid = [sb(f"win_mid{k}", [P, SLOTS, W]) for k in range(2)]
        win_be = [sb(f"win_be{k}", [P, SLOTS, W]) for k in range(2)]
        mid_hi = [sb(f"mid_hi{k}", [P, SLOTS, PADW], F32R) for k in range(2)]
        mid_lo = [sb(f"mid_lo{k}", [P, SLOTS, PADW], F32R) for k in range(2)]
        base_hl = [sb(f"base_hl{k}", [P, SLOTS, PADW], F32R) for k in range(2)]
        last_lh = [sb(f"last_lh{k}", [P, SLOTS, PADW], F32R) for k in range(2)]
        base_hh = [sb(f"base_hh{k}", [P, SLOTS, PADW], F32R) for k in range(2)]
        last_hh = [sb(f"last_hh{k}", [P, SLOTS, PADW], F32R) for k in range(2)]
        gate = sb("gate", [P, 2, 2, N])
        gated = sb("gated", [P, 2, 2, N])
        mixed = sb("mixed", [P, 2, 2, N])
        rows_out = sb("rows_out", [P, HALF, 2, W])

        w_nat = [sb(f"w_nat{k}", [C, C, TAPS, TAPS]) for k in range(2)]
        SECTIONS = ((BASE, MID), (0, BASE), (C - BASE, BASE))
        w_pad = [[sb(f"w_pad{k}_{t}", [C, TAPS, TAPS + 2, n]) for t, (c0, n) in enumerate(SECTIONS)]
                 for k in range(2)]
        w_hi = [[sb(f"w_hi{k}_{t}", [P, TAPS, P], F32R) for t in range(3)] for k in range(2)]
        w_lo = [[sb(f"w_lo{k}_{t}", [P, TAPS, P], F32R) for t in range(3)] for k in range(2)]
        w_two = [[sb(f"w_two{k}_{t}", [P, P], F32R) for t in range(1, 3)] for k in range(2)]
        ident = sb("ident", [C, C])
        prm_rows = sb("prm_rows", [10, P])
        prm = sb("prm", [P, 2, 5])
        veps = sb("veps", [P, 2])
        rvar = sb("rvar", [P, 2])
        rstd0 = sb("rstd0", [P, 2])
        sq = sb("sq", [P, 2])
        corr = sb("corr", [P, 2])
        rstd = sb("rstd", [P, 2])
        inv = sb("inv", [P, 2])
        mi = sb("mi", [P, 2])
        shift = sb("shift", [P, 2])
        gate_bias = sb("gate_bias", [P, 2])

        psum = ctx.enter_context(nc.psum_tensor("acc", [P, 8, BANK], F32))

        w_landed = [sem(f"w_landed{c}") for c in "ab"]
        prm_landed = sem("prm_landed")
        ident_ready = sem("ident_ready")
        wpad_ready = sem("wpad_ready")
        wt_ready = sem("wt_ready")
        whi_ready = sem("whi_ready")
        wlo_ready = sem("wlo_ready")
        prmdup_ready = sem("prmdup_ready")
        prmT_ready = sem("prmT_ready")
        rvar_ready = sem("rvar_ready")
        rstd0_ready = sem("rstd0_ready")
        prm_chain = sem("prm_chain")
        consts_ready = sem("consts_ready")
        rows_zero = sem("rows_zero")
        cols_zero = sem("cols_zero")
        x_landed = sem("x_landed")
        pool_base_landed = sem("pool_base_landed")
        x_early = [sem(f"x_early{i}") for i in range(2)]
        mid_landed = [sem(f"mid_landed{t}") for t in range(2)]
        base_landed = [sem(f"base_landed{t}") for t in range(2)]
        last_landed = [sem(f"last_landed{t}") for t in range(2)]
        hi_ready = [sem(f"hi_ready{c}") for c in "ab"]
        lo_ready = [sem(f"lo_ready{c}") for c in "ab"]
        hh_landed = [[sem(f"hh_landed{t}_{g}") for g in range(2)] for t in range(2)]
        spread_started = sem("spread_started")
        wtwo_ready = sem("wtwo_ready")
        yp_ready = [sem(f"yp_ready{c}") for c in "ab"]
        yr_ready = [sem(f"yr_ready{c}") for c in "ab"]
        gate_ready = [sem(f"gate_ready{c}") for c in "ab"]
        gated_ready = [sem(f"gated_ready{c}") for c in "ab"]
        mixed_ready = [sem(f"mixed_ready{c}") for c in "ab"]
        resid_ready = sem("resid_ready")
        h_ready = sem("h_ready")
        out_ready = sem("out_ready")
        out_stored = [sem(f"out_stored{g}") for g in range(2)]

        def halves(i, g):
            return 2 * i + g + 1

        SPLITS = 4
        def splits(i, g, n=SPLITS):
            return 2 * SPLITS * i + SPLITS * g + n

        WIN_DMAS, HH_DMAS = 4, 2

        def tile_set(k, i):
            turned = isinstance(i, int) and i == (0, B - 1)[k]
            return k if turned else 1 - k

        def landed(k, i, dmas):
            turned = isinstance(i, int) and i == (0, B - 1)[k]
            users = ((1, B)[k] if turned else (i, i + 2)[k])
            return 16 * dmas * users

        def user_before(k, i, inner):
            if not on(i, inner, 1, B - 1 + (k == 0)):
                return None if k == 0 else (0, i)
            return None if k == 0 and not on(i, inner, 2, B) else (k, i - 1)

        def x_at(i):
            start = (i % RING) * (SLOTS * W)
            return x_pair[:, bass.ds(start, SLOTS * W)]

        def weight_parts(t):
            U, L = slice(P // 2, P), slice(0, P // 2)
            return ((slice(0, P), slice(0, P)),) if t == 0 else ((L, L), (U, L))

        def half_slots(g):
            return slice(g * HALF, (g + 1) * HALF)

        def banks(g, kind):
            b = 4 * g + 2 * kind
            return psum[:, b:b + 2, 0:N]

        FIRST, LAST = 0, B + 1

        def steps(eng, body):
            body(0)
            body(1)
            with eng.Fori(2, B - 2) as i:
                body(i, True)
            for i in range(B - 2, B + 2):
                body(i)

        def on(i, inner, low, high):
            return inner or low <= i < high

        def load_windows(eng, k, i, take, row_dims=False, parts=("base", "mid", "last")):
            t = tile_set(k, i)
            for part in parts:
                dst, p0, n, c0, landed_in = {
                    "base": (win_be[t], 0, BASE, 0,
                             pool_base_landed if eng is nc.gpsimd else base_landed[t]),
                    "mid": (win_mid[t], 0, MID, BASE, mid_landed[t]),
                    "last": (win_be[t], P // 2, BASE, C - BASE, last_landed[t])}[part]
                for r in range(4):
                    q = (r + 1) % 2
                    off = (r - 1 - q) // 2
                    lo, hi = max(0, -off), min(SLOTS, SLOTS - off)
                    to = dst[p0 + r * n:p0 + (r + 1) * n, lo:hi, :]
                    eng.dma_start(to if row_dims else to.rearrange("c s w -> c (s w)"),
                                  take(q, c0, n, lo + off, hi + off)).then_inc(landed_in, 16)

        def windows_from(pair):
            return lambda q, c0, n, s0, s1: pair[q * C + c0:q * C + c0 + n, s0 * W:s1 * W]

        def wait_windows_split(eng, k, i, inner):
            before = user_before(k, i, inner)
            if before:
                eng.wait_ge(hi_ready[before[0]], splits(before[1], 1))
                eng.wait_ge(lo_ready[before[0]], splits(before[1], 1))

        def pool_helps(i):
            return isinstance(i, int) and i in (0, B - 1)

        h_flat = h_pair[:].rearrange("p s w -> p (s w)")

        block = ctx.enter_context(nc.Block())

        @block.sync
        def _(sp):
            x_rows = x.rearrange("b c (s q) w -> b q c s w", q=2)
            out_rows = out.rearrange("b c (g s) w -> b g c (s w)", g=2)

            def load_x(i, done=x_landed):
                for q in range(2):
                    dst = x_at(i)[q * C:(q + 1) * C, :].rearrange("c (s w) -> c s w", w=W)
                    src = x_rows[bass.ds(i, 1), q].rearrange("b c s w -> (b c) s w")
                    sp.dma_start(dst, src).then_inc(done, 16)

            def store(i, g):
                sp.wait_ge(out_ready, 2 * halves(i, g))
                dst = out_rows[bass.ds(i, 1), g].rearrange("b c n -> (b c) n")
                sp.dma_start(dst, rows_out[g * C:(g + 1) * C].rearrange("c s q w -> c (s q w)")
                             ).then_inc(out_stored[g], 16)

            for k, w in enumerate((w_a, w_b)):
                sp.dma_start(w_nat[k][:].rearrange("o i a b -> o (i a b)"),
                             w.rearrange("o i a b -> o (i a b)")).then_inc(w_landed[k], 16)
            sp.wait_ge(rows_zero, 1)
            for i in range(2):
                load_windows(sp, 0, i,
                             lambda q, c0, n, s0, s1: x_rows[i, q, c0:c0 + n, s0:s1], True)
            load_x(2)

            def body(i, inner=False):
                if on(i, inner, 1, B - 1):
                    sp.wait_ge(x_landed, 32 * i)
                    wait_windows_split(sp, 0, i + 1, inner)
                    load_windows(sp, 0, i + 1, windows_from(x_at(i + 1)))
                if not inner and i == 1:
                    load_x(0, x_early[0])
                if on(i, inner, 2, B + 2):
                    store(i - 2, 1)
                if on(i, inner, 1, B - 2):
                    if on(i, inner, 2, B):
                        sp.wait_ge(resid_ready, halves(i - 2, 1))
                    load_x(i + 2)
                if on(i, inner, 0, B):
                    sp.wait_ge(h_ready, halves(i, 1))
                    wait_windows_split(sp, 1, i, inner)
                    load_windows(sp, 1, i, windows_from(h_flat),
                                 parts=("mid", "last") if pool_helps(i) else ("base", "mid", "last"))
                if not inner and i == 1:
                    load_x(1, x_early[1])
                if on(i, inner, 1, B + 1):
                    store(i - 1, 0)

            steps(sp, body)
            for g in range(2):
                sp.wait_ge(out_stored[g], 16 * B)

        @block.gpsimd
        def _(pool):
            nc.gpsimd.memset(ident[:], 0.0).then_inc(ident_ready, 1)
            pool.wait_ge(ident_ready, 1)
            nc.gpsimd.affine_select(out=ident[:], in_=ident[:], compare_op=ALU.not_equal, fill=1.0,
                                    base=0, pattern=[[-1, C]], channel_multiplier=1
                                    ).then_inc(ident_ready, 1)
            rows = [theta_a, gamma_a, beta_a, mean_a, var_a, theta_b, gamma_b, beta_b, mean_b, var_b]
            for n, v in enumerate(rows):
                pool.dma_start(prm_rows[n:n + 1, 0:C], v.rearrange("(a c) -> a c", a=1)
                               ).then_inc(prm_landed, 16)

            def spread(k, i):
                t = tile_set(k, i)
                flat_from = last_lh[t][P // 2:P].rearrange("p s w -> p (s w)").bitcast(F32)
                flat_to = last_hh[t][:].rearrange("p s w -> p (s w)").bitcast(F32)
                for g in range(2):
                    a, z = g * HALF * PADW, (g + 1) * HALF * PADW
                    pool.wait_ge(hi_ready[k], splits(i, g, 4))
                    pool.sem_inc(spread_started, 1)
                    for half in range(2):
                        pool.dma_start(flat_to[half * (P // 2):(half + 1) * (P // 2), a:z - 1],
                                       flat_from[:, a + half:z - 1 + half]
                                       ).then_inc(hh_landed[t][g], 16)

            pool.wait_ge(cols_zero, 1)
            spread(0, 0)

            def body(i, inner=False):
                if on(i, inner, 1, B + 1):
                    spread(1, i - 1)
                if on(i, inner, 0, B - 1):
                    spread(0, i + 1)
                if pool_helps(i):
                    pool.wait_ge(h_ready, halves(i, 1))
                    wait_windows_split(pool, 1, i, False)
                    load_windows(nc.gpsimd, 1, i, windows_from(h_flat), parts=("base",))

            steps(pool, body)

        @block.tensor
        def _(pe):
            pe.wait_ge(ident_ready, 2)
            for k in range(2):
                for t, (c0, n) in enumerate(SECTIONS):
                    pe.wait_ge(wpad_ready, 2 * (3 * k + t + 1))
                    for dx in range(TAPS):
                        for q in range(2):
                            last = pe.transpose(
                                psum[0:4 * n, 4 * k + t, (2 * dx + q) * C:(2 * dx + q + 1) * C],
                                w_pad[k][t][:, dx, 1 - q:5 - q, :].rearrange("o r c -> o (r c)"),
                                ident[:])
                    last.then_inc(wt_ready, 1)
            pe.wait_ge(wtwo_ready, 4)

            def conv(k, i, g):
                taps = range(TAPS)
                t = tile_set(k, i)
                mid_h, mid_l, base, last = mid_hi[t], mid_lo[t], base_hl[t], last_lh[t]
                yp = [(base, w_hi[k][1][:, dx], dx) for dx in taps]
                yp += [(base, w_lo[k][1][:, 2], 2), (base_hh[t], w_two[k][0][:], 0)]
                yr = [(mid_h, w_hi[k][0][:, dx], dx) for dx in taps]
                yr += [(mid_h, w_lo[k][0][:, dx], dx) for dx in taps]
                yr += [(mid_l, w_hi[k][0][:, dx], dx) for dx in taps]
                yr += [(last, w_hi[k][2][:, dx], dx) for dx in taps]
                yr += [(last, w_lo[k][2][:, 2], 2), (last_hh[t], w_two[k][1][:], 0)]
                for kind, units, done in ((0, yp, yp_ready[k]), (1, yr, yr_ready[k])):
                    for u, (m, w, dx) in enumerate(units):
                        new = u == 0 or m is not units[u - 1][0]
                        if new and m is not last_hh[t] and m is not mid_l:
                            n = 2 if kind == 0 else 3 if m is mid_h else 4
                            pe.wait_ge(hi_ready[k], splits(i, g, n))
                        if new and m is not last_hh[t] and m is not mid_h:
                            n = 2 if kind == 0 else 3 if m is mid_l else 4
                            pe.wait_ge(lo_ready[k], splits(i, g, n))
                        if m is last_hh[t]:
                            pe.wait_ge(hh_landed[t][g], landed(k, i, HH_DMAS))
                        for b in range(2):
                            s0 = g * HALF + b * BLK
                            mm = pe.matmul(psum[:, 4 * g + 2 * kind + b, 0:N], w,
                                           m[:, s0:s0 + BLK, dx:dx + W],
                                           start=(u == 0), stop=(u == len(units) - 1))
                    mm.then_inc(done, 1)
                    if (isinstance(i, int) and (k, i, g, kind) == (0, 0, 0, 0)):
                        pe.wait_ge(prmdup_ready, 1)
                        pe.transpose(psum[:, 7, 0:10], prm_rows[:, :], ident[0:10, 0:10]
                                     ).then_inc(prmT_ready, 1)

            def body(i, inner=False):
                for g in range(2):
                    if on(i, inner, 0, B):
                        if on(i, inner, 2, B):
                            pe.wait_ge(mixed_ready[1], halves(i - 2, g))
                        elif i == 1:
                            pe.wait_ge(mixed_ready[0], halves(0, g))
                        conv(0, i, g)
                        if not inner and i == 0 and g == 0:
                            pe.wait_ge(wtwo_ready, 8)
                            pe.wait_ge(rvar_ready, 1)
                for g in range(2):
                    if on(i, inner, 1, B + 1):
                        if on(i, inner, 0, B):
                            pe.wait_ge(mixed_ready[0], halves(i, g))
                        else:
                            pe.wait_ge(mixed_ready[1], halves(i - 2, g))
                        conv(1, i - 1, g)

            steps(pe, body)

        @block.scalar
        def _(act):
            def weights_hi(k):
                for t in range(3):
                    act.wait_ge(wt_ready, 3 * k + t + 1)
                    for dst, src in weight_parts(t):
                        nc.scalar.activation(w_hi[k][t][dst].rearrange("p t m -> p (t m)"),
                                             psum[src, 4 * k + t, 0:TAPS * P], ACT.Copy
                                             ).then_inc(whi_ready, 1)

            def split_hi(k, i, g, inner, parts=range(SPLITS)):
                s = half_slots(g)
                U, L = slice(P // 2, P), slice(0, P // 2)
                t = tile_set(k, i)
                before = user_before(k, i, inner)
                if 0 in parts and before:
                    act.wait_ge(yr_ready[before[0]], halves(before[1], g))
                for n in parts:
                    if g == 0 and n == 0:
                        act.wait_ge(base_landed[t], landed(k, i, WIN_DMAS) - (64 if k else 0))
                        if k == 1 and pool_helps(i):
                            act.wait_ge(pool_base_landed, 64 if i == 0 else 128)
                    if g == 0 and n == 2:
                        act.wait_ge(mid_landed[t], landed(k, i, WIN_DMAS))
                    if g == 0 and n == 3:
                        act.wait_ge(last_landed[t], landed(k, i, WIN_DMAS))
                    dst, src = ((base_hl[t][L], win_be[t][L]), (base_hh[t][L], win_be[t][L]),
                                (mid_hi[t][:], win_mid[t][:]), (last_lh[t][U], win_be[t][U]))[n]
                    nc.scalar.activation(dst[:, s, 1:1 + W], src[:, s, :], ACT.Copy
                                         ).then_inc(hi_ready[k], 1)

            def open_gate(k, i, g):
                act.wait_ge(yp_ready[k], halves(i, g))
                nc.scalar.activation(gate[:, g], banks(g, 0), ACT.Sigmoid, scale=ALPHA,
                                     bias=gate_bias[:, k:k + 1]).then_inc(gate_ready[k], 1)

            def norm_h(i, g, inner):
                act.wait_ge(mixed_ready[0], halves(i, g))
                if on(i, inner, 1, B):
                    act.wait_ge(mid_landed[tile_set(1, i - 1)], landed(1, i - 1, WIN_DMAS))
                    act.wait_ge(last_landed[tile_set(1, i - 1)], landed(1, i - 1, WIN_DMAS))
                    act.wait_ge(base_landed[tile_set(1, i - 1)], landed(1, i - 1, WIN_DMAS) - 64)
                    if not inner and i == 1:
                        act.wait_ge(pool_base_landed, 64)
                nc.scalar.activation(h_pair[:, half_slots(g), :].rearrange("p (b s) w -> p b (s w)", b=2),
                                     mixed[:, g], ACT.Relu, scale=inv[:, 0:1],
                                     bias=shift[:, 0:1]).then_inc(h_ready, 1)

            def finish(i, g, inner):
                act.wait_ge(resid_ready, halves(i, g))
                if on(i, inner, 1, B):
                    act.wait_ge(out_stored[g], 16 * i)
                for q in range(2):
                    nc.scalar.activation(
                        rows_out[g * C:(g + 1) * C, :, q, :],
                        gated[q * C:(q + 1) * C, g].rearrange("c b (s w) -> c (b s) w", w=W),
                        ACT.Relu, bias=shift[q * C:(q + 1) * C, 1:2]).then_inc(out_ready, 1)

            weights_hi(0)
            act.wait_ge(cols_zero, 1)
            split_hi(0, 0, 0, False)
            weights_hi(1)
            split_hi(0, 0, 1, False)
            act.wait_ge(rvar_ready, 2)
            nc.scalar.activation(rstd0[:], rvar[:], ACT.Sqrt).then_inc(rstd0_ready, 1)
            act.wait_ge(consts_ready, 1)

            def body(i, inner=False):
                a, b = on(i, inner, 0, B), on(i, inner, 1, B + 1)
                if not inner and i == 0:
                    for g in range(2):
                        open_gate(0, 0, g)
                        split_hi(0, 1, g, False)
                        norm_h(0, g, False)
                    return
                for g in range(2):
                    nxt = (1, i - 1, g) if b and (inner or i < B or g) else None
                    if nxt:
                        split_hi(*nxt, inner, range(3))
                    if a:
                        open_gate(0, i, g)
                    if g == 0 and on(i, inner, 2, B + 2):
                        finish(i - 2, 1, inner)
                    if g == 1 and a:
                        norm_h(i, 0, inner)
                    if nxt:
                        split_hi(*nxt, inner, [3])
                for g in range(2):
                    nxt = (0, i + 1, g) if on(i, inner, 1, B - 1) else None
                    if nxt:
                        split_hi(*nxt, inner, range(3))
                    if b:
                        open_gate(1, i - 1, g)
                    if g == 0 and a:
                        norm_h(i, 1, inner)
                    if g == 1 and b:
                        finish(i - 1, 0, inner)
                    if nxt:
                        split_hi(*nxt, inner, [3])
                if not inner and i == B - 1:
                    split_hi(1, i, 0, False)

            steps(act, body)

        @block.vector
        def _(dve):
            for k in range(2):
                for t in (win_mid[k], win_be[k]):
                    for s in (0, SLOTS - 1):
                        last = nc.vector.memset(t[:, s, :], 0.0)
            last.then_inc(rows_zero, 1)
            for k in range(2):
                for t in (mid_hi[k], mid_lo[k], base_hl[k], last_lh[k], base_hh[k]):
                    last = nc.vector.memset(t[:, :, 0:PADW:PADW - 1].bitcast(F32), 0.0)
            last.then_inc(cols_zero, 1)
            for k in range(2):
                dve.wait_ge(w_landed[k], 16)
                for t, (c0, n) in enumerate(SECTIONS):
                    nc.vector.memset(w_pad[k][t][:, :, 0:5:4, :], 0.0).then_inc(wpad_ready, 1)
                    nc.vector.tensor_copy(w_pad[k][t][:, :, 1:4, :],
                                          w_nat[k][:, c0:c0 + n].rearrange("o i a b -> o b a i")
                                          ).then_inc(wpad_ready, 1)

            def weights_lo(k):
                made = 0
                for t in range(3):
                    made += len(weight_parts(t))
                    dve.wait_ge(whi_ready, 5 * k + made)
                    for dst, src in weight_parts(t):
                        hi = w_hi[k][t][dst].rearrange("p t m -> p (t m)")
                        nc.vector.tensor_tensor(w_lo[k][t][dst].rearrange("p t m -> p (t m)"),
                                                psum[src, 4 * k + t, 0:TAPS * P], hi.bitcast(F32),
                                                ALU.subtract).then_inc(wlo_ready, 1)
                dve.wait_ge(wlo_ready, 5 * (k + 1))
                for t in range(1, 3):
                    for h in range(2):
                        part = slice(h * (P // 2), (h + 1) * (P // 2))
                        nc.vector.tensor_copy(w_two[k][t - 1][part], w_lo[k][t][part, h].bitcast(F32)
                                              ).then_inc(wtwo_ready, 1)

            chain = [0]

            def link(ins):
                chain[0] += 1
                ins.then_inc(prm_chain, 1)
                dve.wait_ge(prm_chain, chain[0])

            def batch_norms():
                dve.wait_ge(prmT_ready, 1)
                nc.vector.tensor_copy(prm[:].rearrange("p k n -> p (k n)"), psum[:, 7, 0:10]
                                      ).then_inc(rvar_ready, 1)
                dve.wait_ge(rvar_ready, 1)
                theta, gamma, beta, mean, var = (prm[:, :, n] for n in range(5))
                link(nc.vector.tensor_scalar(veps[:], var, EPS, None, ALU.add))
                nc.vector.reciprocal(rvar[:], veps[:]).then_inc(rvar_ready, 1)
                dve.wait_ge(rstd0_ready, 1)
                link(nc.vector.tensor_tensor(sq[:], rstd0[:], rstd0[:], ALU.mult))
                link(nc.vector.tensor_tensor(corr[:], sq[:], veps[:], ALU.mult))
                link(nc.vector.tensor_scalar(corr[:], corr[:], -0.5, 1.5, ALU.mult, ALU.add))
                link(nc.vector.tensor_tensor(rstd[:], rstd0[:], corr[:], ALU.mult))
                link(nc.vector.tensor_tensor(inv[:], gamma, rstd[:], ALU.mult))
                link(nc.vector.tensor_tensor(mi[:], mean, inv[:], ALU.mult))
                link(nc.vector.tensor_tensor(shift[:], beta, mi[:], ALU.subtract))
                nc.vector.tensor_scalar(gate_bias[:], theta, -ALPHA, None, ALU.mult
                                        ).then_inc(consts_ready, 1)

            def split_lo(k, i, g):
                s = half_slots(g)
                t = tile_set(k, i)
                mid, be = win_mid[t], win_be[t]
                U, L = slice(P // 2, P), slice(0, P // 2)
                for n, dst, src, hi in ((1, base_hl[t][U], be[L], base_hl[t][L]),
                                        (2, base_hh[t][U], be[L], None),
                                        (3, mid_lo[t][:], mid[:], mid_hi[t][:]),
                                        (4, last_lh[t][L], be[U], last_lh[t][U])):
                    if hi is None:
                        nc.vector.tensor_copy(dst[:, s, 0:W], src[:, s, :]).then_inc(lo_ready[k], 1)
                        continue
                    dve.wait_ge(hi_ready[k], splits(i, g, n))
                    nc.vector.tensor_tensor(dst[:, s, 1:1 + W], src[:, s, :],
                                            hi[:, s, 1:1 + W].bitcast(F32), ALU.subtract
                                            ).then_inc(lo_ready[k], 1)

            def mix(k, i, g, inner):
                dve.wait_ge(gate_ready[k], halves(i, g))
                dve.wait_ge(yr_ready[k], halves(i, g))
                if k == 0:
                    if on(i, inner, 2, B):
                        dve.wait_ge(out_ready, 2 * halves(i - 2, g))
                else:
                    if on(i, False, B - 1, B) and not inner:
                        dve.wait_ge(out_ready, 2 * halves(i - 1, g))
                nc.vector.tensor_tensor(gated[:, g], gate[:, g], banks(g, 1), ALU.mult
                                        ).then_inc(gated_ready[k], 1)
                dve.wait_ge(gated_ready[k], halves(i, g))
                if k == 1:
                    dve.wait_ge(h_ready, halves(i + 1, g) if (inner or i + 1 < B) else 2 * B)
                nc.vector.tensor_tensor(mixed[:, g], gated[:, g], banks(g, 0), ALU.add
                                        ).then_inc(mixed_ready[k], 1)
                if k == 1:
                    if isinstance(i, int) and i == 0:
                        dve.wait_ge(x_early[0], 32)
                    dve.wait_ge(mixed_ready[1], halves(i, g))
                    xs = x_at(i).rearrange("p (g b n) -> p g b n", g=2, b=2)[:, g]
                    nc.vector.scalar_tensor_tensor(gated[:, g], mixed[:, g], inv[:, 1:2], xs,
                                                   ALU.mult, ALU.add).then_inc(resid_ready, 1)

            weights_lo(0)
            dve.wait_ge(cols_zero, 1)
            split_lo(0, 0, 0)
            dve.wait_ge(prm_landed, 160)
            nc.vector.tensor_copy(prm_rows[:, C:P], prm_rows[:, 0:C]).then_inc(prmdup_ready, 1)
            weights_lo(1)
            split_lo(0, 0, 1)
            batch_norms()

            def body(i, inner=False):
                a, b = on(i, inner, 0, B), on(i, inner, 1, B + 1)
                if not inner and i == 0:
                    for g in range(2):
                        mix(0, 0, g, False)
                        split_lo(0, 1, g)
                    return
                for g in range(2):
                    if g == 0 and on(i, inner, 2, B + 2):
                        mix(1, i - 2, 1, inner)
                    if g == 1 and a:
                        mix(0, i, 0, inner)
                    if b and (inner or i < B or g):
                        split_lo(1, i - 1, g)
                for g in range(2):
                    if g == 0 and a:
                        mix(0, i, 1, inner)
                    if g == 1 and b:
                        mix(1, i - 1, 0, inner)
                    if on(i, inner, 1, B - 1):
                        split_lo(0, i + 1, g)
                if not inner and i == B - 1:
                    split_lo(1, i, 0)

            steps(dve, body)


_PARAMS = [f"L0_conv_{n}_{c}" for c in "ab" for n in ("w", "theta", "gamma", "beta", "mean", "var")]
_INS = ["x"] + _PARAMS


def kernel(**inputs):
    import numpy as _np
    import concourse.bacc as _bacc
    from concourse import mybir as _mybir
    from concourse.bass_utils import run_bass_kernel_spmd as _run

    nc = _bacc.Bacc("TRN2", target_bir_lowering=False, num_devices=1)
    arrays, args = {}, []
    for name in _INS:
        a = _np.ascontiguousarray(inputs[name])
        arrays[f"in_{name}_dram"] = a
        args.append(nc.dram_tensor(f"in_{name}_dram", a.shape, _mybir.dt.from_np(a.dtype), kind="ExternalInput").ap())
    shape = inputs["x"].shape
    args.append(nc.dram_tensor("out_0_dram", shape, _mybir.dt.from_np(_np.dtype("float32")), kind="ExternalOutput").ap())
    gated_conv_pair_kernel(nc, *args)
    r = _run(nc, [arrays], core_ids=[0])
    return r.results[0]["out_0_dram"]
```
